# Optimizing a Trainium2 kernel written in Bass

```python
import numpy as np
import jax
import jax.numpy as jnp

def _softmax(x, axis=-1):
    return jax.nn.softmax(x, axis=axis)

def _gelu(x):
    return jax.nn.gelu(x, approximate=True)

def _silu(x):
    return jax.nn.silu(x)

def _sigmoid(x):
    return jax.nn.sigmoid(x)

def _layernorm(x, axis=-1, eps=1e-05):
    m = jnp.mean(x, axis=axis, keepdims=True)
    v = jnp.var(x, axis=axis, keepdims=True)
    return (x - m) / jnp.sqrt(v + eps)

def _scatter_add(tgt, idx, src, axis=0):
    return tgt.at[idx].add(src)

def _segment_sum(src, seg, n):
    return jax.ops.segment_sum(src, seg, n)
kernel_name = 'mk_prb_d2_jaxref_r8_13e44b'

def setup_inputs(seed: int=0):
    np.random.seed(seed)
    _w = jnp.asarray

    def _L0_attn_setup():
        import jax, jax.numpy as jnp
        import numpy as np
        N_HEADS = 16
        NEG = -10000.0
        key = jax.random.key(seed)
        k1, k2, k3 = jax.random.split(key, 3)
        B, S, E = (4, 256, 256)
        x = jax.random.normal(k1, (B, S, E), dtype=jnp.float32)
        w_qkv = jax.random.normal(k2, (E, 3 * E), dtype=jnp.float32) * E ** (-0.5)
        w_out = jax.random.normal(k3, (E, E), dtype=jnp.float32) * E ** (-0.5)
        return {'x': x, 'w_qkv': w_qkv, 'w_out': w_out}
    _L0_attn_in = _L0_attn_setup()

    def _L0_ffn_setup():
        import jax, jax.numpy as jnp
        import numpy as np
        DIM = 256
        HID = 704
        ZERO_POINT = 128.0

        def _qlinear(x, wq, scale):
            W = (wq.astype(jnp.float32) - ZERO_POINT) * scale[:, None]
            return jnp.einsum('bsd,hd->bsh', x, W)
        key = jax.random.key(seed)
        ks = jax.random.split(key, 7)
        B, S = (4, 256)
        sg = jax.random.uniform(ks[1], (HID,)) * (0.02 / np.sqrt(DIM)) + 0.0001
        su = jax.random.uniform(ks[3], (HID,)) * (0.02 / np.sqrt(DIM)) + 0.0001
        sd = jax.random.uniform(ks[5], (DIM,)) * (0.02 / np.sqrt(HID)) + 0.0001
        return {'x': jax.random.normal(ks[0], (B, S, DIM), dtype=jnp.float32), 'wq_gate': jax.random.randint(ks[2], (HID, DIM), 0, 32, dtype=jnp.int32), 's_gate': sg, 'wq_up': jax.random.randint(ks[4], (HID, DIM), 0, 32, dtype=jnp.int32), 's_up': su, 'wq_down': jax.random.randint(ks[6], (DIM, HID), 0, 32, dtype=jnp.int32), 's_down': sd}
    _L0_ffn_in = _L0_ffn_setup()

    def _L1_attn_setup():
        import jax, jax.numpy as jnp
        import numpy as np
        B, S, E, H, L = (2, 256, 256, 16, 64)
        HD = E // H

        def _reference_tuple_inner(x, Wq, Wdkv, Wuk, Wuv, ln_g, ln_b, Wo_h, Wo, bo):
            Bx, Sx, Ex = x.shape
            xh = x.reshape(Bx, Sx, H, HD).transpose(0, 2, 1, 3)
            c = jnp.einsum('bhsd,hld->bhsl', xh, Wdkv)
            mu = c.mean(-1, keepdims=True)
            var = c.var(-1, keepdims=True)
            c = (c - mu) * jax.lax.rsqrt(var + 1e-05)
            c = c * ln_g[None, :, None, :] + ln_b[None, :, None, :]
            absorbed = jnp.einsum('hij,hlj->hil', Wq, Wuk)
            q_lat = jnp.einsum('bhsd,hdl->bhsl', xh, absorbed)
            scores = jnp.einsum('bhsl,bhtl->bhst', q_lat, c)
            scores = scores * (1.0 / np.sqrt(L).astype(np.float32))
            mask = jnp.tril(jnp.ones((Sx, Sx), dtype=bool))
            scores = jnp.where(mask, scores, -jnp.inf)
            w = jax.nn.softmax(scores, axis=-1)
            v = jnp.einsum('bhsl,hld->bhsd', c, Wuv)
            oh = jnp.einsum('bhst,bhtd->bhsd', w, v)
            oh = jnp.einsum('bhsd,hed->bhse', oh, Wo_h)
            o = oh.transpose(0, 2, 1, 3).reshape(Bx, Sx, Ex)
            out = o @ Wo.T + bo
            return (out, c)
        key = jax.random.key(seed)
        ks = jax.random.split(key, 8)
        sd = 0.02
        return {'x': jax.random.normal(ks[0], (B, S, E), jnp.float32), 'Wq': jax.random.normal(ks[1], (H, HD, HD), jnp.float32) * sd, 'Wdkv': jax.random.normal(ks[2], (H, L, HD), jnp.float32) * sd, 'Wuk': jax.random.normal(ks[3], (H, L, HD), jnp.float32) * sd, 'Wuv': jax.random.normal(ks[4], (H, L, HD), jnp.float32) * sd, 'ln_g': jnp.ones((H, L), jnp.float32), 'ln_b': jnp.zeros((H, L), jnp.float32), 'Wo_h': jax.random.normal(ks[5], (H, HD, HD), jnp.float32) * sd, 'Wo': jax.random.normal(ks[6], (E, E), jnp.float32) * sd, 'bo': jnp.zeros((E,), jnp.float32)}
    _L1_attn_in = _L1_attn_setup()

    def _L1_ffn_setup():
        import jax, jax.numpy as jnp
        import numpy as np
        HID = 256
        N_EXP = 32
        F_EXP = 96
        TOP_K = 6
        F_SH = 192
        B, S = (1, 128)
        key = jax.random.key(seed)
        ks = jax.random.split(key, 8)
        s = 0.02
        return {'hidden_states': jax.random.normal(ks[0], (B, S, HID), dtype=jnp.float32), 'gate_w': jax.random.normal(ks[1], (HID, N_EXP), dtype=jnp.float32) * s, 'wg': jax.random.normal(ks[2], (N_EXP, HID, F_EXP), dtype=jnp.float32) * s, 'wu': jax.random.normal(ks[3], (N_EXP, HID, F_EXP), dtype=jnp.float32) * s, 'wd': jax.random.normal(ks[4], (N_EXP, F_EXP, HID), dtype=jnp.float32) * s, 'sg': jax.random.normal(ks[5], (HID, F_SH), dtype=jnp.float32) * s, 'su': jax.random.normal(ks[6], (HID, F_SH), dtype=jnp.float32) * s, 'sd': jax.random.normal(ks[7], (F_SH, HID), dtype=jnp.float32) * s}
    _L1_ffn_in = _L1_ffn_setup()
    _d = {'L0_attn_x': _L0_attn_in['x'], 'L0_attn_w_qkv': _L0_attn_in['w_qkv'], 'L0_attn_w_out': _L0_attn_in['w_out'], 'L0_ffn_wq_gate': _L0_ffn_in['wq_gate'], 'L0_ffn_s_gate': _L0_ffn_in['s_gate'], 'L0_ffn_wq_up': _L0_ffn_in['wq_up'], 'L0_ffn_s_up': _L0_ffn_in['s_up'], 'L0_ffn_wq_down': _L0_ffn_in['wq_down'], 'L0_ffn_s_down': _L0_ffn_in['s_down'], 'L1_attn_Wq': _L1_attn_in['Wq'], 'L1_attn_Wdkv': _L1_attn_in['Wdkv'], 'L1_attn_Wuk': _L1_attn_in['Wuk'], 'L1_attn_Wuv': _L1_attn_in['Wuv'], 'L1_attn_ln_g': _L1_attn_in['ln_g'], 'L1_attn_ln_b': _L1_attn_in['ln_b'], 'L1_attn_Wo_h': _L1_attn_in['Wo_h'], 'L1_attn_Wo': _L1_attn_in['Wo'], 'L1_attn_bo': _L1_attn_in['bo'], 'L1_ffn_gate_w': _L1_ffn_in['gate_w'], 'L1_ffn_wg': _L1_ffn_in['wg'], 'L1_ffn_wu': _L1_ffn_in['wu'], 'L1_ffn_wd': _L1_ffn_in['wd'], 'L1_ffn_sg': _L1_ffn_in['sg'], 'L1_ffn_su': _L1_ffn_in['su'], 'L1_ffn_sd': _L1_ffn_in['sd']}
    _x0 = _d['L0_attn_x']
    _d['L0_attn_x'] = jax.random.normal(jax.random.fold_in(jax.random.key(seed), 1), (16, 256, 256), dtype=_x0.dtype)
    del _x0
    return _d

def reference(L0_attn_x, L0_attn_w_qkv, L0_attn_w_out, L0_ffn_wq_gate, L0_ffn_s_gate, L0_ffn_wq_up, L0_ffn_s_up, L0_ffn_wq_down, L0_ffn_s_down, L1_attn_Wq, L1_attn_Wdkv, L1_attn_Wuk, L1_attn_Wuv, L1_attn_ln_g, L1_attn_ln_b, L1_attn_Wo_h, L1_attn_Wo, L1_attn_bo, L1_ffn_gate_w, L1_ffn_wg, L1_ffn_wu, L1_ffn_wd, L1_ffn_sg, L1_ffn_su, L1_ffn_sd):

    def _L0_attn_ref(x, w_qkv, w_out):
        import jax, jax.numpy as jnp
        import numpy as np
        N_HEADS = 16
        NEG = -10000.0
        B, S, E = x.shape
        H = N_HEADS
        D = E // H
        qkv = x @ w_qkv
        q, k, v = jnp.split(qkv, 3, axis=-1)
        q = q.reshape(B, H, S, D)
        k = k.reshape(B, H, S, D)
        v = v.reshape(B, H, S, D)
        qk = jnp.einsum('bhqd,bhkd->bhqk', q, k) / D ** 0.5
        tri = jnp.tril(jnp.ones((S, S), dtype=bool))
        causal = jnp.where(tri, jnp.float32(1.0), jnp.float32(NEG))
        qk = qk + causal
        attn = jax.nn.softmax(qk, axis=-1)
        o = jnp.einsum('bhqk,bhkd->bhqd', attn, v)
        o = o.reshape(B, S, E)
        return o @ w_out

    def _L0_ffn_ref(x, wq_gate, s_gate, wq_up, s_up, wq_down, s_down):
        import jax, jax.numpy as jnp
        import numpy as np
        DIM = 256
        HID = 704
        ZERO_POINT = 128.0

        def _qlinear(x, wq, scale):
            W = (wq.astype(jnp.float32) - ZERO_POINT) * scale[:, None]
            return jnp.einsum('bsd,hd->bsh', x, W)
        gate = _qlinear(x, wq_gate, s_gate)
        gate = jax.nn.silu(gate)
        up = _qlinear(x, wq_up, s_up)
        return _qlinear(gate * up, wq_down, s_down)

    def _L1_attn_ref(x, Wq, Wdkv, Wuk, Wuv, ln_g, ln_b, Wo_h, Wo, bo):
        import jax, jax.numpy as jnp
        import numpy as np
        B, S, E, H, L = (2, 256, 256, 16, 64)
        HD = E // H

        def _reference_tuple_inner(x, Wq, Wdkv, Wuk, Wuv, ln_g, ln_b, Wo_h, Wo, bo):
            Bx, Sx, Ex = x.shape
            xh = x.reshape(Bx, Sx, H, HD).transpose(0, 2, 1, 3)
            c = jnp.einsum('bhsd,hld->bhsl', xh, Wdkv)
            mu = c.mean(-1, keepdims=True)
            var = c.var(-1, keepdims=True)
            c = (c - mu) * jax.lax.rsqrt(var + 1e-05)
            c = c * ln_g[None, :, None, :] + ln_b[None, :, None, :]
            absorbed = jnp.einsum('hij,hlj->hil', Wq, Wuk)
            q_lat = jnp.einsum('bhsd,hdl->bhsl', xh, absorbed)
            scores = jnp.einsum('bhsl,bhtl->bhst', q_lat, c)
            scores = scores * (1.0 / np.sqrt(L).astype(np.float32))
            mask = jnp.tril(jnp.ones((Sx, Sx), dtype=bool))
            scores = jnp.where(mask, scores, -jnp.inf)
            w = jax.nn.softmax(scores, axis=-1)
            v = jnp.einsum('bhsl,hld->bhsd', c, Wuv)
            oh = jnp.einsum('bhst,bhtd->bhsd', w, v)
            oh = jnp.einsum('bhsd,hed->bhse', oh, Wo_h)
            o = oh.transpose(0, 2, 1, 3).reshape(Bx, Sx, Ex)
            out = o @ Wo.T + bo
            return (out, c)
        return _reference_tuple_inner(x, Wq, Wdkv, Wuk, Wuv, ln_g, ln_b, Wo_h, Wo, bo)[0]

    def _L1_ffn_ref(hidden_states, gate_w, wg, wu, wd, sg, su, sd):
        import jax, jax.numpy as jnp
        import numpy as np
        HID = 256
        N_EXP = 32
        F_EXP = 96
        TOP_K = 6
        F_SH = 192
        B, S = (1, 128)
        orig_shape = hidden_states.shape
        x = hidden_states.reshape(-1, HID)
        scores = jax.nn.sigmoid(x @ gate_w)
        topk_w, topk_i = jax.lax.top_k(scores, TOP_K)
        topk_w = topk_w / (jnp.sum(topk_w, axis=-1, keepdims=True) + 1e-20)
        combine = jnp.sum(jax.nn.one_hot(topk_i, N_EXP, dtype=topk_w.dtype) * topk_w[..., None], axis=1)
        g = jnp.einsum('td,edf->tef', x, wg)
        u = jnp.einsum('td,edf->tef', x, wu)
        act = jax.nn.silu(g) * u
        routed = jnp.einsum('tef,efd,te->td', act, wd, combine)
        routed = routed.reshape(orig_shape)
        shared = jax.nn.silu(hidden_states @ sg) * (hidden_states @ su) @ sd
        return routed + shared
    x = L0_attn_x
    xn = _layernorm(x, axis=-1)
    x = x + _L0_attn_ref(xn, L0_attn_w_qkv, L0_attn_w_out) + _L0_ffn_ref(xn, L0_ffn_wq_gate, L0_ffn_s_gate, L0_ffn_wq_up, L0_ffn_s_up, L0_ffn_wq_down, L0_ffn_s_down)
    xn = _layernorm(x, axis=-1)
    x = x + _L1_attn_ref(xn, L1_attn_Wq, L1_attn_Wdkv, L1_attn_Wuk, L1_attn_Wuv, L1_attn_ln_g, L1_attn_ln_b, L1_attn_Wo_h, L1_attn_Wo, L1_attn_bo) + _L1_ffn_ref(xn, L1_ffn_gate_w, L1_ffn_wg, L1_ffn_wu, L1_ffn_wd, L1_ffn_sg, L1_ffn_su, L1_ffn_sd)
    return x

_drawn_inputs = setup_inputs


def setup_inputs(seed=0):
    import zlib

    import numpy as np

    out = dict(_drawn_inputs(seed))
    spreads = {'L1_attn_ln_g': (1.0, 0.6), 'L1_attn_ln_b': (0.0, 0.8), 'L1_attn_bo': (0.0, 0.657)}
    factors = {'L0_ffn_s_gate': 8.0,
     'L0_ffn_s_up': 8.0,
     'L0_ffn_s_down': 8.0,
     'L1_attn_Wq': 8.0,
     'L1_attn_Wdkv': 8.0,
     'L1_attn_Wuk': 8.0,
     'L1_attn_Wuv': 8.0,
     'L1_attn_Wo_h': 8.0,
     'L1_attn_Wo': 8.0,
     'L1_ffn_gate_w': 8.0,
     'L1_ffn_wg': 8.0,
     'L1_ffn_wu': 8.0,
     'L1_ffn_wd': 8.0,
     'L1_ffn_sg': 4.033,
     'L1_ffn_su': 3.967,
     'L1_ffn_sd': 3.967}
    for name, (base, spread) in spreads.items():
        noise = np.random.default_rng([zlib.crc32(name.encode()), seed]).standard_normal(out[name].shape)
        drawn = base * np.exp(spread * noise) if base else spread * noise
        out[name] = jnp.asarray(drawn.astype(out[name].dtype))
    for name, factor in factors.items():
        out[name] = (out[name] * factor).astype(out[name].dtype)
    return out
```

```python
from contextlib import ExitStack

import numpy as np

import concourse.bass as bass
from concourse import mybir

F32 = mybir.dt.float32
F16 = mybir.dt.float16
BF16 = mybir.dt.bfloat16
I32 = mybir.dt.int32
ALU = mybir.AluOpType
ACT = mybir.ActivationFunctionType
AX = mybir.AxisListType

P = 128
EPS = 1e-5
CODE_ZERO = 128.0
L0_MASKED = -10000.0
BIG = 1.0e30

PER = {
    "x1_loaded": 16, "part1_saved": 16, "v1_saved": 16, "land1_loaded0": 48, "land1_loaded1": 48, "va1_loaded": 512,
    "max1_placed": 16, "o1_saved": 256, "ot1_loaded": 16, "out_saved": 16, "part2_saved": 16, "stack2_loaded": 96,
    "comb_saved": 16, "cb2_loaded": 192, "max2_placed": 16, "gc2_made": 12, "ln1_root": 1, "x1h_made": 1,
    "part1_high": 2, "th1_made": 6, "h1h_made": 6, "o1h_made": 1, "ln2_root": 1, "x2_parts": 2, "root2": 2,
    "k2h_made": 2, "o2h_made": 1, "th2_made": 14, "h2h_made": 14, "ln1": 8, "h1l_made": 6, "stack1_made": 2,
    "acc1_free": 4, "y1_made": 1, "rc1_made": 2, "ln2": 8, "xb2_made": 1, "rs2_made": 2, "va2_made": 2,
    "part2_made": 2, "router": 14, "rc2_made": 2, "acc2_free": 3, "h2l_made": 14, "down1_done": 6, "p1_used": 16,
    "acc1_full": 1, "p2_used": 16, "down2_done": 14, "acc2_full": 1,
}
CREDIT = {
    "acc1_free": 1, "stack1_made": 1, "part1_saved": 1, "v1_saved": 1, "h1l_made": 2, "down1_done": 2, "p1_used": 2,
    "p2_used": 2, "h2l_made": 2, "down2_done": 2, "out_saved": 1, "gc2_made": 1, "acc2_free": 1,
}


class Before:

    def __init__(self, it):
        self.it = it


TURNS = ([1, 0] * 2 + [1, 1, 0] + [1] * 17 + [0] + [1] * 8 + [0] + [1] * 11 + [0, 0, 0, 0, 1] * 4 + [0, 1, 0, 0]
         + [0, 0, 0, 1] * 5 + [0, 0, 1, 1, 1, 0])


def program(nc, a, out):
    B, S, E = a["L0_attn_x"].shape
    T, K = S // P, E // P
    HID = a["L0_ffn_wq_gate"].shape[0]
    NCH = (HID + P - 1) // P
    CH_M = [min(P, HID - P * c) for c in range(NCH)]
    H, HD, _ = a["L1_attn_Wq"].shape
    L = a["L1_attn_Wdkv"].shape[1]
    NX, _, FX = a["L1_ffn_wg"].shape
    FS = a["L1_ffn_sg"].shape[1]
    FS2 = FS - P
    TOP = 6
    R8 = 8
    C = E // HD
    PAIRS = NX * FX // P // 2
    LAND = 1
    QK0, QK1 = 3 * HD + 3, 3 * HD + 1
    HG = H // 2

    ctx = ExitStack()
    with ctx:
        def sb(name, shape, dt=F32):
            return ctx.enter_context(nc.sbuf_tensor(name, shape, dt))

        def bank(name):
            return ctx.enter_context(nc.psum_tensor(name, [P, 512], F32))

        def scratch(name, shape, dt=F32):
            return nc.dram_tensor(name, shape, dt, kind="Internal").ap()

        sems = {}

        def sem(name):
            if name not in sems:
                sems[name] = ctx.enter_context(nc.semaphore(name))
            return sems[name]

        def event(name, it, n):
            if it is None:
                return sem(name), n
            if isinstance(it, Before):
                n, it = n - PER[name], it.it
            return sem(name), it * PER[name] + (n + CREDIT.get(name, 0))

        def carry(eng, name):
            eng.sem_inc(sem(name), 1)

        wqkv = [sb(f"wqkv{i}", [P, K, 3 * E], F16) for i in range(2)]
        wout = [sb(f"wout{i}", [P, K, E], F16) for i in range(2)]
        wo = [sb(f"wo{i}", [P, K, E], F16) for i in range(2)]
        wgate = sb("wgate", [P, K, HID], F16)
        wup = sb("wup", [P, K, HID], F16)
        wdown = sb("wdown", [P, NCH, E], F16)
        xg = [sb(f"xg{i}", [P, K, NX * FX], F16) for i in range(2)]
        xu = [sb(f"xu{i}", [P, K, NX * FX], F16) for i in range(2)]
        xd = [sb(f"xd{i}", [P, 2 * PAIRS, E], F16) for i in range(2)]
        shg = [sb(f"shg{i}", [P, K, FS], F16) for i in range(2)]
        shu = [sb(f"shu{i}", [P, K, FS], F16) for i in range(2)]
        shd = [sb(f"shd{i}", [P, 2, E], F16) for i in range(2)]
        rout = [sb(f"rout{i}", [P, K, NX], F16) for i in range(2)]
        fold = [sb(f"fold{i}", [P, K, 3, P], F16) for i in range(2)]
        sg_half = sb("sg_half", [P, NCH])
        su_half = sb("su_half", [P, NCH])
        sd_row = sb("sd_row", [P, E])
        bo_row = sb("bo_row", [P, E])
        key_const = sb("key_const", [P, K])
        val_const = sb("val_const", [P, E])
        ident = sb("ident", [P, P])
        ident16 = sb("ident16", [P, P], F16)
        identb = sb("identb", [P, P], BF16)
        same_head = sb("same_head", [P, 8, HD])
        head_mean = sb("head_mean", [P, P])
        head_mean8 = sb("head_mean8", [P, 8])
        maskq0 = sb("maskq0", [P, 2, S], F16)
        maskq1 = sb("maskq1", [P, S], BF16)
        maskk0 = sb("maskk0", [P, P], F16)
        maskk1 = sb("maskk1", [P, P], BF16)
        one64 = sb("one64", [L, P])
        centre = sb("centre", [L, L])

        x1 = sb("x1", [P, T, E])
        st1 = sb("st1", [P, T, 6])
        mv1 = sb("mv1", [P, T, 2])
        xn1 = sb("xn1", [P, T, E])
        x1h = sb("x1h", [P, K, S], F16)
        x1l = sb("x1l", [P, K, S], F16)
        part1 = sb("part1", [P, 4, K, S], F16)
        qst1 = sb("qst1", [QK0, C, S], F16)
        kst1 = sb("kst1", [QK0, C, S], F16)
        land1 = [sb(f"land1{i}", [3 * HD, C, S], F16) for i in range(LAND)]
        va1 = sb("va1", [P, T, H, HD + 1])
        junk1 = sb("junk1", [P, 2, 2, S], BF16)
        mx1 = sb("mx1", [P, H, T])
        mt1 = sb("mt1", [2 * H, P], F16)
        p1 = sb("p1", [P, 2, 2, S])
        rc1 = sb("rc1", [P, HG, 2])
        th1 = sb("th1", [P, 2, S])
        gs1 = sb("gs1", [P, 2, S])
        h1h = sb("h1h", [P, 2, S], F16)
        h1l = sb("h1l", [P, 2, S], F16)

        v1 = ot1 = xn1
        o1h, o1l = part1[:, 0], part1[:, 1]
        h1 = th1
        on1 = th1[:, :, :].rearrange("p a b -> p (a b)").rearrange("p (h j d) -> p h j d", h=H, j=T)
        y1 = x1

        x2 = sb("x2", [P, T, E])
        st2 = sb("st2", [P, T, 6])
        mv2 = sb("mv2", [P, T, 2])
        xn2 = sb("xn2", [P, T, E])
        x2f = sb("x2f", [P, K, S])
        part2 = sb("part2", [P, 4, K, S], F16)
        x2h, x2l = part2[:, 0], part2[:, 1]
        pr2 = sb("pr2", [P, K, S])
        rt2 = sb("rt2", [P, T, H])
        va2 = sb("va2", [P, T, H, HD + 1])
        mx2 = sb("mx2", [P, H, T])
        mt2 = sb("mt2", [2 * H, P], F16)
        rc2 = sb("rc2", [P, HG, 2])
        el2 = sb("el2", [P, T, NX])
        sc2 = sb("sc2", [P, T, NX + 8])
        m82 = sb("m82", [P, T, 8])
        rp2 = sb("rp2", [P, T, NX + 8])
        ws2 = sb("ws2", [P, T])
        cm2 = sb("cm2", [P, T, NX])
        cb2 = sb("cb2", [P, 2 * PAIRS, S])
        th2 = sb("th2", [P, 2, 2 * S])
        gs2 = sb("gs2", [P, 2, 2 * S])
        h2h = sb("h2h", [P, 2, 2 * S], F16)
        h2l = sb("h2l", [P, 2, 2 * S], F16)
        xb2 = x2
        rs2 = x2f
        kf2 = pr2
        ct2 = pr2[0:NX, 0, :]
        on2 = xn2[:, :, :].rearrange("p t (h d) -> p t h d", h=H)
        xo2 = xn2
        o2h, o2l = part2[:, 2], part2[:, 3]
        gc2 = gs2
        qst2, kst2, junk2 = qst1, kst1, junk1
        p2 = p1[:, :, :, :].rearrange("p s k q -> p s (k q)")[:, :, 0:3 * P]

        NST = 4
        stage = [cb2[:, 6 * i:6 * i + 6, :].rearrange("p a b -> p (a b)") for i in range(NST)]
        codes = [gs1[:, i, :].bitcast(I32) for i in range(2)]
        code_f = [x1[:, i, :] for i in range(2)]
        th2f, gs2f = (x[:, :, :].rearrange("p a b -> p (a b)") for x in (th2, gs2))
        wq_bd, wo_bd = (th2f[:, E * i:E * i + E].rearrange("p (k n) -> p k n", k=K) for i in range(2))
        f_t, f_a, f_m = th2f[:, 2 * E:4 * E], gs2f[:, 0:2 * E], gs2f[:, 2 * E:4 * E]
        wuk, wuv, wdkv = xn2[0:L, 0, :], xn2[0:L, 1, :], pr2[0:L, 0, :]
        ln_g, ln_b = pr2[0:L, 1, 0:H], pr2[0:L, 1, H:2 * H]
        b_w, g_w = x2[0:L, 0, :], x2[0:L, 1, :]
        wo_nat = x2f
        order = [th1[:, 0, 0:P], th1[:, 0, P:2 * P]]
        order_i = [th1[:, 1, 0:P].bitcast(I32), th1[:, 1, P:2 * P].bitcast(I32)]
        pos = [rc1[:, 0, 0:1], rc1[:, 0, 1:2]]
        mask_tmp = xn1[:, 0, 0:P], xn1[:, 0, P:2 * P], xn1[:, 1, 0:P], xn1[:, 1, P:2 * P]

        def row_tile(i):
            t = xd[i // 4][32 * (i % 4):32 * (i % 4) + 1, 0:C * S // E, :]
            return t.rearrange("r a b -> r (a b)")

        ring1 = [bank("s1a"), bank("s1b")]
        acc1 = bank("s1acc")
        ring2 = [bank(f"s2r{i}") for i in range(4)]
        acc2 = bank("s2acc")

        part1_d = scratch("part1_d", [B, 4, E, S], F16)
        part2_d = scratch("part2_d", [B, 4, E, S], F16)
        v_d = scratch("v_d", [B, S, E])
        o_d = scratch("o_d", [B, S, E])
        comb_d = scratch("comb_d", [B, NX, S])

        def wide(x):
            return x.rearrange("(k p) n -> p k n", p=P)

        pieces = [
            (wide(a["L0_attn_w_qkv"]), [w[:, :, :] for w in wqkv], K * 3 * E),
            (wide(a["L0_attn_w_out"]), [w[:, :, :] for w in wout], K * E),
            (wide(a["L1_ffn_gate_w"]), [w[:, :, :] for w in rout], K * NX),
            (wide(a["L1_ffn_sg"]), [w[:, :, :] for w in shg], K * FS),
            (wide(a["L1_ffn_su"]), [w[:, :, :] for w in shu], K * FS),
            (a["L1_ffn_sd"][0:P, :], [w[:, 0, :] for w in shd], E),
            (a["L1_ffn_sd"][P:FS, :], [w[0:FS2, 1, :] for w in shd], E),
        ]
        for k in range(K):
            for e0 in range(0, NX, 16):
                for src, dst in ((a["L1_ffn_wg"], xg), (a["L1_ffn_wu"], xu)):
                    pieces.append((src[e0:e0 + 16, k * P:(k + 1) * P, :].rearrange("e p f -> p e f"),
                                   [w[:, k, e0 * FX:(e0 + 16) * FX].rearrange("p (e f) -> p e f", f=FX)
                                    for w in dst], 16 * FX))
        wd_v = a["L1_ffn_wd"].rearrange("e f d -> (e f) d").rearrange("(c p) d -> p c d", p=P)
        for c0 in range(0, 2 * PAIRS, 6):
            pieces.append((wd_v[:, c0:c0 + 6, :], [w[:, c0:c0 + 6, :] for w in xd], 6 * E))

        def staged(i, n, like):
            v = stage[i % NST][0:like.shape[0], 0:n]
            if len(like.shape) == 3:
                v = v.rearrange("p (a b) -> p a b", a=like.shape[1])
            return v

        NCODE = 2 * NCH + 2 * 3
        SMALL = 16 * (2 * H + 5 + 1 + 4 + 2)
        FD = 10

        U1 = {"x": 0, "q": 1, "k": 2, "v": 3, "ffn_a": 4, "q_rows": 10, "max": 26, "ffn_b": 27, "k_rows": 33, "o": 49}
        N1 = 50
        U2 = {"x": 0, "gram": 1, "var": 2, "var_t": 3, "k": 4, "v": 5, "logit": 6, "comb": 7, "q_rows": 8,
              "max": 24, "k_rows": 25, "o": 41, "unit": 42}
        UNITS = 2 + PAIRS
        N2 = U2["unit"] + 2 * UNITS
        for b in range(2):
            PER[f"ring1_full{b}"] = PER[f"ring1_free{b}"] = len(range(b, N1, 2))
            CREDIT[f"ring1_free{b}"] = 1
        for b in range(4):
            PER[f"ring2_full{b}"] = PER[f"ring2_free{b}"] = len(range(b, N2, 4))
            CREDIT[f"ring2_free{b}"] = 1

        def ffn_use(c):
            return U1["ffn_a"] + 2 * c if c < 3 else U1["ffn_b"] + 2 * (c - 3)

        def free1(it, n):
            return event(f"ring1_free{n % 2}", it, n // 2)

        def full1(it, n):
            return event(f"ring1_full{n % 2}", it, n // 2 + 1)

        def emptied1(it, n):
            return event(f"ring1_free{n % 2}", it, n // 2 + 1)

        def free2(it, n):
            return event(f"ring2_free{n % 4}", it, n // 4)

        def full2(it, n):
            return event(f"ring2_full{n % 4}", it, n // 4 + 1)

        def emptied2(it, n):
            return event(f"ring2_free{n % 4}", it, n // 4 + 1)

        def fills1(n):
            return sem(f"ring1_full{n % 2}")

        def empties1(n):
            return sem(f"ring1_free{n % 2}")

        def fills2(n):
            return sem(f"ring2_full{n % 4}")

        def empties2(n):
            return sem(f"ring2_free{n % 4}")

        def two(x):
            return x[:, 0:512].rearrange("p (a b) -> p a b", a=2)

        def one(x, it):
            if isinstance(it, Before):
                return x[bass.ds(it.it - 1, 1)]
            return x[it:it + 1] if isinstance(it, int) else x[bass.ds(it, 1)]

        block = ctx.enter_context(nc.Block())

        def run(layer1, layer0):
            for turn in TURNS:
                stages = (layer0, layer1)[turn]
                if stages is not None:
                    next(stages, None)
            for stages in (layer0, layer1):
                assert stages is None or next(stages, "end") == "end"

        def sp1(sp, it):
            sp.wait_ge(*event("acc1_free", it, 0))
            sp.dma_start(x1[:, :, :], one(a["L0_attn_x"], it).rearrange("b (t p) e -> p (b t) e", p=P)).then_inc(sem("x1_loaded"), 16)
            sp.wait_ge(*emptied1(it, U1["q"]))
            carry(sp, "sp_waited")
            sp.wait_ge(*emptied1(it, U1["k"]))
            sp.dma_start(one(part1_d, it).rearrange("b g (k p) s -> p (b g k) s", p=P),
                              part1[:, :, :, :].rearrange("p g k s -> p (g k) s")).then_inc(sem("part1_saved"), 16)
            sp.wait_ge(*emptied1(it, U1["v"]))
            sp.dma_start(one(v_d, it).rearrange("b (t p) e -> p (b t) e", p=P), v1[:, :, :]).then_inc(sem("v1_saved"), 16)
            sp.wait_ge(*event("part1_saved", it, 16))
            for n, (first, parts) in enumerate(((0, (0, 0, 1)), (2, (0, 1, 0)))):
                sp.wait_ge(*event("stack1_made", it, n + 1 - LAND))
                for g, which in enumerate(parts):
                    sp.dma_start(land1[n % LAND][g * HD:(g + 1) * HD, :, :],
                                      one(part1_d, it)[:, first + which].rearrange("b (c d) s -> d (b c) s", d=HD)).then_inc(sem(f"land1_loaded{n}"), 16)
            sp.wait_ge(*event("v1_saved", it, 16))
            vv = one(v_d, it).rearrange("b (h j r) (c d) -> j c r (b h) d", j=2, r=R8, d=HD)
            for c in range(C):
                for j in range(T):
                    sp.dma_start(va1[c * R8:(c + 1) * R8, j, :, 0:HD], vv[j, c]).then_inc(sem("va1_loaded"), 16)
            sp.wait_ge(*emptied1(it, U1["max"]))
            sp.dma_start(qst1[48:49, :, :].rearrange("o h (j q) -> o (h j) q", q=P), mt1[:, :]).then_inc(sem("max1_placed"), 16)
            sp.wait_ge(*event("acc1_free", it, 3))
            ov = one(o_d, it).rearrange("b (g r) (c d) -> c r (b g) d", r=R8, d=HD)
            for c in range(C):
                sp.dma_start(ov[c], on1[c * R8:(c + 1) * R8, :, :, :].rearrange("p h j d -> p (h j) d")).then_inc(sem("o1_saved"), 16)
            sp.wait_ge(*event("o1_saved", it, 16 * C))
            sp.dma_start(ot1[:, :, :], one(o_d, it).rearrange("b (t p) e -> p (b t) e", p=P)).then_inc(sem("ot1_loaded"), 16)

        def save_out(sp, it):
            sp.wait_ge(*event("acc2_free", it, 3))
            sp.dma_start(one(out, it).rearrange("b (t p) e -> p (b t) e", p=P), xo2[:, :, :]).then_inc(sem("out_saved"), 16)

        @block.sync
        def _(sp):
            for name, n in CREDIT.items():
                sp.sem_inc(sem(name), n)
            count = 0

            def small(dst, src, slow=False):
                nonlocal count
                count += 16
                sp.dma_start(dst, src, allow_slow_non_contiguous=slow).then_inc(sem("small_loaded"), 16)

            sp.wait_ge(*event("cleared", None, 2))
            for h in range(H):
                r, k = (h % 8) * HD, h // 8
                small(wq_bd[r:r + HD, k, r:r + HD], a["L1_attn_Wq"][h])
                small(wo_bd[r:r + HD, k, r:r + HD], a["L1_attn_Wo_h"][h])
            for dst, name in ((wuk, "L1_attn_Wuk"), (wuv, "L1_attn_Wuv"), (wdkv, "L1_attn_Wdkv")):
                small(dst.rearrange("l (h j) -> l h j", h=H), a[name].rearrange("h l j -> l h j"))
            small(ln_g, a["L1_attn_ln_g"].rearrange("h l -> l h"), slow=True)
            small(ln_b, a["L1_attn_ln_b"].rearrange("h l -> l h"), slow=True)
            small(wo_nat[:, :, :], wide(a["L1_attn_Wo"]))
            for dst, name in ((sg_half, "L0_ffn_s_gate"), (su_half, "L0_ffn_s_up")):
                whole = P * (NCH - 1)
                small(dst[:, 0:NCH - 1], a[name][0:whole].rearrange("(c p) -> p c", p=P), slow=True)
                small(dst[0:CH_M[-1], NCH - 1:NCH], a[name][whole:HID].rearrange("(p c) -> p c", c=1), slow=True)
            small(sd_row[:, :], a["L0_ffn_s_down"].partition_broadcast(P))
            small(bo_row[:, :], a["L1_attn_bo"].partition_broadcast(P))
            assert count == SMALL, count

            for i in range(NCODE):
                if i >= 2:
                    sp.wait_ge(*event("codes_used", None, i - 1))
                if i < 2 * NCH:
                    c, m = i // 2, CH_M[i // 2]
                    src = a[("L0_ffn_wq_gate", "L0_ffn_wq_up")[i % 2]][P * c:P * c + m, :]
                    dst = codes[i % 2][0:m, :]
                else:
                    m, c = (i - 2 * NCH) // 3, (i - 2 * NCH) % 3
                    n = min(2 * P, HID - 2 * P * c)
                    src = a["L0_ffn_wq_down"][P * m:P * m + P, 2 * P * c:2 * P * c + n]
                    dst = codes[i % 2][:, 0:n]
                sp.dma_start(dst, src).then_inc(sem(f"codes_loaded{i % 2}"), 16)

            sp.wait_ge(*event("rows_made", None, 10))
            for dst, row, i in ((kst1, 48, 0), (kst1, 49, 1), (kst1, 50, 2), (qst1, 49, 3), (qst1, 50, 4)):
                sp.dma_start(dst[row:row + 1, :, :].rearrange("r c s -> r (c s)"), row_tile(i)).then_inc(sem("rows_placed"), 16)

            for i, (src, dst, n) in enumerate(pieces):
                if i >= NST:
                    sp.wait_ge(*event("stage_free", None, i - NST + 1))
                if i == len(pieces) - 4:
                    sp.wait_ge(*event("rows_placed", None, 80))
                sp.dma_start(staged(i, n, dst[0]), src).then_inc(sem(f"staged{i % NST}"), 16)

            sp1(sp, 0)
            with sp.Fori(1, B) as it:
                sp1(sp, it)
                save_out(sp, Before(it))
            save_out(sp, B - 1)
            sp.wait_ge(*event("out_saved", None, 16 * B + CREDIT.get("out_saved", 0)))

        def gp2(gp, it):
            g = nc.gpsimd
            gp.wait_ge(*event("part2_made", it, 2))
            carry(gp, "gp_waited")
            gp.dma_start(one(part2_d, it).rearrange("b g (k p) s -> p (b g k) s", p=P),
                              part2[:, :, :, :].rearrange("p g k s -> p (g k) s")).then_inc(sem("part2_saved"), 16)
            gp.wait_ge(*event("part2_saved", it, 16))
            gp.wait_ge(*event("p1_used", it, H))
            carry(gp, "gp_waited")
            for st, first, parts in ((qst2, 0, (0, 0, 1)), (kst2, 2, (0, 1, 0))):
                for gr, which in enumerate(parts):
                    gp.dma_start(st[gr * HD:(gr + 1) * HD, :, :],
                                      one(part2_d, it)[:, first + which].rearrange("b (c d) s -> d (b c) s", d=HD)).then_inc(sem("stack2_loaded"), 16)
            gp.wait_ge(*emptied2(it, U2["comb"]))
            carry(gp, "gp_waited")
            gp.dma_start(one(comb_d, it).rearrange("b e s -> (b e) s"), ct2).then_inc(sem("comb_saved"), 16)
            gp.wait_ge(*event("comb_saved", it, 16))
            carry(gp, "gp_waited")
            src = one(comb_d, it).rearrange("b (a f) s -> f (b a) s", f=4)
            for i in range(3):
                for q in range(4):
                    dst = cb2[32 * q:32 * q + 32, :, :].rearrange("p (a i) s -> p a i s", i=3)[:, :, i, :]
                    gp.dma_start(dst, src[(4 * i + q) // 3].partition_broadcast(32)).then_inc(sem("cb2_loaded"), 16)
            gp.wait_ge(*emptied2(it, U2["max"]))
            carry(gp, "gp_waited")
            gp.dma_start(qst2[48:49, :, :].rearrange("o h (t q) -> o (h t) q", q=P), mt2[:, :]).then_inc(sem("max2_placed"), 16)
            gp.wait_ge(*event("cb2_loaded", it, 16 * 12))
            for p in range(PAIRS):
                gp.wait_ge(*emptied2(it, U2["unit"] + 2 * (p + 2)))
                g.tensor_tensor(gc2[:, p % 2, :], gs2[:, p % 2, :],
                                     cb2[:, 2 * p:2 * p + 2, :].rearrange("p a s -> p (a s)"), ALU.mult).then_inc(sem("gc2_made"), 1)

        @block.gpsimd
        def _(gp):
            g = nc.gpsimd
            g.memset(wq_bd, 0.0).then_inc(sem("cleared"), 1)
            g.memset(wo_bd, 0.0).then_inc(sem("cleared"), 1)
            g.memset(ident[:, :], 0.0).then_inc(sem("gp_const"), 1)
            g.memset(same_head[:, :, :], 1.0).then_inc(sem("gp_const"), 1)
            gp.wait_ge(*event("gp_const", None, 2))
            g.affine_select(out=ident[:, :], in_=ident[:, :], pattern=[[-1, P]], compare_op=ALU.not_equal,
                                 fill=1.0, base=0, channel_multiplier=1).then_inc(sem("gp_const"), 1)
            g.affine_select(out=same_head[:, :, :], in_=same_head[:, :, :], pattern=[[-HD, 8], [0, HD]],
                                 compare_op=ALU.is_ge, fill=0.0, base=0, channel_multiplier=1).then_inc(sem("gp_const"), 1)
            gp.wait_ge(*event("gp_const", None, 4))
            g.affine_select(out=same_head[:, :, :], in_=same_head[:, :, :], pattern=[[HD, 8], [0, HD]],
                                 compare_op=ALU.is_ge, fill=0.0, base=HD - 1, channel_multiplier=-1).then_inc(sem("gp_const"), 1)
            g.memset(one64[:, :], 1.0).then_inc(sem("gp_const"), 1)
            g.iota(order_i[0], pattern=[[1, C], [C, R8]], base=0, channel_multiplier=0).then_inc(sem("gp_const"), 1)
            g.iota(order_i[1], pattern=[[1, P]], base=0, channel_multiplier=0).then_inc(sem("gp_const"), 1)
            g.memset(va1[:, :, :, HD:HD + 1], 1.0).then_inc(sem("gp_const"), 1)
            g.memset(va2[:, :, :, HD:HD + 1], 1.0).then_inc(sem("gp_const"), 1)
            g.memset(sc2[:, :, NX:NX + 4], 2.0).then_inc(sem("gp_const"), 1)
            g.memset(sc2[:, :, NX + 4:NX + 8], 3.0).then_inc(sem("gp_const"), 1)
            for i, vals in enumerate(((1.0, 1.0), (0.0, 1.0), (1.0, 0.0), (4 * L0_MASKED, 0.0), (0.0, 4.0))):
                r = row_tile(i).rearrange("o (h j q) -> o h j q", j=2, q=P)
                for j in range(2):
                    if i + j:
                        gp.wait_ge(*event("rows_made", None, 2 * i + j))
                    else:
                        gp.wait_ge(*event("gp_const", None, 12))
                    g.memset(r[:, :, j, :], vals[j]).then_inc(sem("rows_made"), 1)
            with gp.Fori(0, B) as it:
                gp2(gp, it)

        def root(act, it, mv, name):
            act.wait_ge(*event(name, it, 5))
            nc.scalar.sqrt(mv[:, :, 1], mv[:, :, 1]).then_inc(sem(name + "_root"), 1)

        def act1(act, it):
            s = nc.scalar
            root(act, it, mv1, "ln1")
            act.wait_ge(*full1(it, U1["x"]))
            bk = ring1[U1["x"] % 2]
            s.copy(x1h[:, :, :], two(bk)).then_inc(sem("x1h_made"), 1)
            yield
            act.wait_ge(*event("part1_saved", it, 0))
            for i, u in enumerate(("q", "k")):
                act.wait_ge(*full1(it, U1[u]))
                bk = ring1[U1[u] % 2]
                s.copy(part1[:, 2 * i, :, :], two(bk)).then_inc(sem("part1_high"), 1)
            yield
            act.wait_ge(*full1(it, U1["v"]))
            bk = ring1[U1["v"] % 2]
            act.wait_ge(*event("v1_saved", it, 0))
            s.copy(v1[:, :, :], two(bk)).then_inc(empties1(U1["v"]), 1)
            for c in range(NCH):
                if c == 3:
                    for h in range(H):
                        yield
                m = CH_M[c]
                act.wait_ge(*full1(it, ffn_use(c)))
                bk = ring1[(ffn_use(c)) % 2]
                act.wait_ge(*event("h1l_made", it, c - 1))
                s.activation(th1[0:m, c % 2, :], bk[0:m, 0:S], ACT.Tanh, scale=sg_half[0:m, c:c + 1]).then_inc(sem("th1_made"), 1)
                act.wait_ge(*emptied1(it, ffn_use(c) + 1))
                act.wait_ge(*event("down1_done", it, c - 1))
                s.copy(h1h[0:m, c % 2, :], h1[0:m, c % 2, :]).then_inc(sem("h1h_made"), 1)
                yield
            for h in range(H):
                act.wait_ge(*full1(it, U1["k_rows"] + h))
                bk = ring1[(U1["k_rows"] + h) % 2]
                act.wait_ge(*event("p1_used", it, h - 1))
                s.activation(p1[:, h % 2, :, :], two(bk), ACT.Exp, scale=HD ** -0.5).then_inc(empties1(U1["k_rows"] + h), 1)
                yield
            yield
            act.wait_ge(*full1(it, U1["o"]))
            bk = ring1[U1["o"] % 2]
            s.copy(o1h, two(bk)).then_inc(sem("o1h_made"), 1)

        def act2(act, it):
            s = nc.scalar
            root(act, it, mv2, "ln2")
            act.wait_ge(*full2(it, U2["x"]))
            bk = ring2[U2["x"] % 4]
            s.copy(x2h, two(bk)).then_inc(sem("x2_parts"), 1)
            s.copy(x2f[:, :, :], two(bk)).then_inc(sem("x2_parts"), 1)
            yield
            act.wait_ge(*emptied2(it, U2["var"]))
            s.sqrt(rs2[:, :, :], rs2[:, :, :]).then_inc(sem("root2"), 1)
            act.wait_ge(*emptied2(it, U2["var_t"]))
            s.sqrt(rt2[:, :, :], rt2[:, :, :]).then_inc(sem("root2"), 1)
            yield
            act.wait_ge(*emptied2(it, U2["k"]))
            for k in range(K):
                s.activation(part2[:, 2, k, :], kf2[:, k, :], ACT.Identity, bias=key_const[:, k:k + 1]).then_inc(sem("k2h_made"), 1)
            act.wait_ge(*full2(it, U2["logit"]))
            bk = ring2[U2["logit"] % 4]
            s.activation(el2[:, :, :], bk[:, 0:T * NX].rearrange("p (t e) -> p t e", t=T), ACT.Exp, scale=-1.0).then_inc(empties2(U2["logit"]), 1)
            yield
            act.wait_ge(*full2(it, U2["comb"]))
            bk = ring2[U2["comb"] % 4]
            s.copy(ct2, bk[0:NX, 0:S]).then_inc(empties2(U2["comb"]), 1)
            yield
            for h in range(H + 1):
                yield
            for h in range(H):
                act.wait_ge(*full2(it, U2["k_rows"] + h))
                bk = ring2[(U2["k_rows"] + h) % 4]
                act.wait_ge(*event("p2_used", it, h - 1))
                s.activation(p2[:, h % 2, :], bk[:, 0:3 * P], ACT.Exp, scale=L ** -0.5).then_inc(empties2(U2["k_rows"] + h), 1)
                yield
            yield
            act.wait_ge(*full2(it, U2["o"]))
            bk = ring2[U2["o"] % 4]
            s.copy(o2h, two(bk)).then_inc(sem("o2h_made"), 1)
            for n in range(UNITS + 1):
                if n < UNITS:
                    m, w = unit(n)
                    act.wait_ge(*full2(it, U2["unit"] + 2 * n))
                    bk = ring2[(U2["unit"] + 2 * n) % 4]
                    act.wait_ge(*event("h2l_made", it, n - 1))
                    s.activation(th2[0:m, n % 2, 0:w], bk[0:m, 0:w], ACT.Tanh, scale=0.5).then_inc(sem("th2_made"), 1)
                if n >= 1:
                    m, w = unit(n - 1)
                    act.wait_ge(*emptied2(it, U2["unit"] + 2 * (n - 1) + 1))
                    act.wait_ge(*event("down2_done", it, n - 2))
                    s.copy(h2h[0:m, (n - 1) % 2, 0:w], th2[0:m, (n - 1) % 2, 0:w]).then_inc(sem("h2h_made"), 1)
                if n < UNITS:
                    yield

        def unit(n):
            return (P, S) if n == 0 else (FS2, S) if n == 1 else (P, 2 * S)

        @block.scalar
        def _(act):
            s = nc.scalar
            for i in range(NCODE):
                act.wait_ge(*event("codes_turned", None, i + 1))
                bk = ring1[i % 2]
                if i < 2 * NCH:
                    c, m = i // 2, CH_M[i // 2]
                    s.copy((wgate, wup)[i % 2][:, :, P * c:P * c + m], two(bk)[:, :, 0:m]).then_inc(sem("codes_kept"), 1)
                else:
                    m, c = (i - 2 * NCH) // 3, (i - 2 * NCH) % 3
                    if c < 2:
                        s.copy(wdown[:, 2 * c:2 * c + 2, P * m:P * m + P], two(bk)[:, :, 0:P]).then_inc(sem("codes_kept"), 1)
                    else:
                        s.copy(wdown[:, 4, P * m:P * m + P], bk[:, 0:P])
                        s.copy(wdown[0:CH_M[-1], 5, P * m:P * m + P], bk[0:CH_M[-1], 256:256 + P]).then_inc(sem("codes_kept"), 1)
            for k in range(K):
                act.wait_ge(*event("fold_dve", None, FD * k + 7))
                s.copy(fold[0][:, k, :, :].rearrange("p a b -> p (a b)"), f_m[:, 0:3 * P]).then_inc(sem("fold_act"), 1)
            act.wait_ge(*event("fold_pe", None, 3 * K + 1))
            s.copy(wo[0][:, :, :], two(ring2[0])).then_inc(sem("fold_act"), 1)
            act.wait_ge(*event("rows_placed", None, 80))
            for i, (src, dst, n) in enumerate(pieces):
                act.wait_ge(*event(f"staged{i % NST}", None, 16 * (i // NST + 1)))
                s.copy(dst[0], staged(i, n, dst[0])).then_inc(sem("high_made"), 1)
            run(None, act1(act, 0))
            with act.Fori(1, B) as it:
                run(act2(act, Before(it)), act1(act, it))
            run(act2(act, B - 1), None)

        def code_size(i):
            if i < 2 * NCH:
                return CH_M[i // 2], E
            return P, min(2 * P, HID - 2 * P * ((i - 2 * NCH) % 3))

        def layernorm(dve, it, x, st, mv, xn, name):
            v = nc.vector
            for t in range(T):
                v.bn_stats(st[:, t, :], x[:, t, :]).then_inc(sem(name), 1)
            dve.wait_ge(*event(name, it, 2))
            carry(dve, "dve_waited")
            for t in range(T):
                v.bn_aggr(mv[:, t, :], st[:, t, :]).then_inc(sem(name), 1)
            dve.wait_ge(*event(name, it, 4))
            v.tensor_scalar(mv[:, :, 1], mv[:, :, 1], EPS, None, ALU.add).then_inc(sem(name), 1)
            dve.wait_ge(*event(name + "_root", it, 1))
            v.reciprocal(mv[:, :, 1], mv[:, :, 1]).then_inc(sem(name), 1)
            dve.wait_ge(*event(name, it, 6))
            for t in range(T):
                v.tensor_scalar(xn[:, t, :], x[:, t, :], mv[:, t, 0:1], mv[:, t, 1:2], ALU.subtract, ALU.mult).then_inc(sem(name), 1)

        def normalise(dve, it, acc, half, rc, outs, name):
            v = nc.vector
            view = acc[:, 0:HG * 2 * (HD + 1)].rearrange("p (h j d) -> p h j d", h=HG, j=2)
            v.reciprocal(rc[:, :, :], view[:, :, :, HD]).then_inc(sem(name), 1)
            dve.wait_ge(*event(name, it, half + 1))
            for n, j in enumerate(range(T)):
                yield n, v.tensor_tensor(outs[j], view[:, :, j, 0:HD], rc[:, :, j:j + 1].to_broadcast([P, HG, HD]), ALU.mult)

        def dve1(dve, it):
            v = nc.vector
            dve.wait_ge(*event("x1_loaded", it, 16))
            layernorm(dve, it, x1, st1, mv1, xn1, "ln1")
            dve.wait_ge(*full1(it, U1["x"]))
            bk = ring1[U1["x"] % 2]
            dve.wait_ge(*event("x1h_made", it, 1))
            v.tensor_tensor(x1l[:, :, :], two(bk), x1h[:, :, :], ALU.subtract).then_inc(empties1(U1["x"]), 1)
            yield
            for i, u in enumerate(("q", "k")):
                dve.wait_ge(*full1(it, U1[u]))
                bk = ring1[U1[u] % 2]
                dve.wait_ge(*event("part1_high", it, i + 1))
                v.tensor_tensor(part1[:, 2 * i + 1, :, :], two(bk), part1[:, 2 * i, :, :], ALU.subtract).then_inc(empties1(U1[u]), 1)
            yield
            for c in range(3):
                dve_ffn1(dve, it, c)
                yield
            dve.wait_ge(*event("p2_used", it, 0))
            for n, st in enumerate((qst1, kst1)):
                dve.wait_ge(*event(f"land1_loaded{n}", it, 48))
                for j in range(T):
                    o = st[0:3 * HD, :, P * j:P * j + P].bitcast(F32).rearrange("p h (c r) -> p h c r", c=C)
                    i = land1[n % LAND][:, :, :].bitcast(F32).rearrange("p c (h j r) -> p j h c r", h=H, j=2)[:, j]
                    ins = v.tensor_copy(o, i)
                ins.then_inc(sem("stack1_made"), 1)
            for h in range(H):
                dve.wait_ge(*full1(it, U1["q_rows"] + h))
                bk = ring1[(U1["q_rows"] + h) % 2]
                if h >= 2:
                    dve.wait_ge(*emptied1(it, U1["q_rows"] + h - 2))
                carry(dve, "dve_waited")
                for j in range(T):
                    ins = v.tensor_tensor_reduce(junk1[:, h % 2, j, :], bk[:, S * j:S * j + S], maskq0[:, j, :], 1.0, -3.0e38,
                                                 ALU.add, ALU.max, mx1[:, h, j:j + 1])
                ins.then_inc(empties1(U1["q_rows"] + h), 1)
                yield
            dve.wait_ge(*full1(it, U1["max"]))
            bk = ring1[U1["max"] % 2]
            v.tensor_scalar(mt1[:, :], bk[0:2 * H, 0:P], -1.0, None, ALU.mult).then_inc(empties1(U1["max"]), 1)
            for c in range(3, NCH):
                dve_ffn1(dve, it, c)
                yield
            dve.wait_ge(*event("down1_done", it, NCH))
            v.tensor_tensor(gs1[:, :, :], two(acc1), sd_row[:, :].unsqueeze(1).to_broadcast([P, T, E]), ALU.mult).then_inc(sem("acc1_free"), 1)
            dve.wait_ge(*event("acc1_free", it, 1))
            v.tensor_tensor(y1[:, :, :], gs1[:, :, :], x1[:, :, :], ALU.add).then_inc(sem("y1_made"), 1)
            for h in range(HG):
                yield
            for half in range(2):
                dve.wait_ge(*event("p1_used", it, HG * (half + 1)))
                hs = slice(HG * half, HG * half + HG)
                for n, ins in normalise(dve, it, acc1, half, rc1, [on1[:, hs, j, :] for j in range(T)], "rc1_made"):
                    if n == T - 1:
                        ins.then_inc(sem("acc1_free"), 1)
                if half == 0:
                    for h in range(HG, H):
                        yield
            yield
            dve.wait_ge(*full1(it, U1["o"]))
            bk = ring1[U1["o"] % 2]
            dve.wait_ge(*event("o1h_made", it, 1))
            v.tensor_tensor(o1l, two(bk), o1h, ALU.subtract).then_inc(empties1(U1["o"]), 1)
            dve.wait_ge(*event("acc1_full", it, 1))
            dve.wait_ge(*event("acc2_free", it, 0))
            v.tensor_tensor(x2[:, :, :], two(acc1), y1[:, :, :], ALU.add).then_inc(sem("acc1_free"), 1)

        def dve_ffn1(dve, it, c):
            v, m, s = nc.vector, CH_M[c], c % 2
            dve.wait_ge(*event("th1_made", it, c + 1))
            bk = ring1[ffn_use(c) % 2]
            v.scalar_tensor_tensor(gs1[0:m, s, :], th1[0:m, s, :], 1.0, bk[0:m, 0:S], ALU.add, ALU.mult).then_inc(empties1(ffn_use(c)), 1)
            dve.wait_ge(*full1(it, ffn_use(c) + 1))
            bk = ring1[(ffn_use(c) + 1) % 2]
            dve.wait_ge(*emptied1(it, ffn_use(c)))
            v.scalar_tensor_tensor(h1[0:m, s, :], bk[0:m, 0:S], su_half[0:m, c:c + 1], gs1[0:m, s, :],
                                            ALU.mult, ALU.mult).then_inc(empties1(ffn_use(c) + 1), 1)
            dve.wait_ge(*event("h1h_made", it, c + 1))
            v.tensor_tensor(h1l[0:m, s, :], h1[0:m, s, :], h1h[0:m, s, :], ALU.subtract).then_inc(sem("h1l_made"), 1)

        def dve2(dve, it):
            v = nc.vector
            dve.wait_ge(*event("acc1_free", it, 4))
            dve.wait_ge(*event("out_saved", it, 0))
            layernorm(dve, it, x2, st2, mv2, xn2, "ln2")
            dve.wait_ge(*event("ln2", it, 8))
            v.tensor_tensor(xb2[:, :, :], x2[:, :, :], bo_row[:, :].unsqueeze(1).to_broadcast([P, T, E]), ALU.add).then_inc(sem("xb2_made"), 1)
            dve.wait_ge(*full2(it, U2["x"]))
            bk = ring2[U2["x"] % 4]
            dve.wait_ge(*event("x2_parts", it, 2))
            v.tensor_tensor(x2l, two(bk), x2h, ALU.subtract).then_inc(empties2(U2["x"]), 1)
            yield
            dve.wait_ge(*full2(it, U2["gram"]))
            bk = ring2[U2["gram"] % 4]
            v.tensor_tensor(pr2[:, :, :], two(bk), x2f[:, :, :], ALU.mult).then_inc(empties2(U2["gram"]), 1)
            dve.wait_ge(*full2(it, U2["var"]))
            bk = ring2[U2["var"] % 4]
            v.tensor_scalar(rs2[:, :, :], two(bk), 0.0, EPS, ALU.max, ALU.add).then_inc(empties2(U2["var"]), 1)
            dve.wait_ge(*full2(it, U2["var_t"]))
            bk = ring2[U2["var_t"] % 4]
            v.tensor_scalar(rt2[:, :, :], bk[:, 0:T * H].rearrange("p (t h) -> p t h", t=T), 0.0, EPS, ALU.max, ALU.add).then_inc(empties2(U2["var_t"]), 1)
            yield
            dve.wait_ge(*event("root2", it, 2))
            v.reciprocal(rs2[:, :, :], rs2[:, :, :]).then_inc(sem("rs2_made"), 1)
            v.reciprocal(rt2[:, :, :], rt2[:, :, :]).then_inc(sem("rs2_made"), 1)
            dve.wait_ge(*event("rs2_made", it, 2))
            dve.wait_ge(*full2(it, U2["k"]))
            bk = ring2[U2["k"] % 4]
            v.tensor_tensor(kf2[:, :, :], two(bk), rs2[:, :, :], ALU.mult).then_inc(empties2(U2["k"]), 1)
            dve.wait_ge(*full2(it, U2["v"]))
            bk = ring2[U2["v"] % 4]
            for t in range(T):
                ins = v.tensor_tensor(va2[:, t, :, 0:HD], bk[:, S * t:S * t + S].rearrange("p (h d) -> p h d", h=H),
                                      rt2[:, t, :].unsqueeze(2).to_broadcast([P, H, HD]), ALU.mult)
            ins.then_inc(empties2(U2["v"]), 1)
            dve.wait_ge(*emptied2(it, U2["v"]))
            for t in range(T):
                v.tensor_tensor(va2[:, t, :, 0:HD], va2[:, t, :, 0:HD], val_const[:, :].rearrange("p (h d) -> p h d", h=H),
                                     ALU.add).then_inc(sem("va2_made"), 1)
            dve.wait_ge(*event("k2h_made", it, 2))
            for k in range(K):
                v.scalar_tensor_tensor(part2[:, 3, k, :], kf2[:, k, :], key_const[:, k:k + 1], part2[:, 2, k, :],
                                            ALU.add, ALU.subtract).then_inc(sem("part2_made"), 1)
            yield
            dve.wait_ge(*emptied2(it, U2["logit"]))
            rs = "router"
            v.tensor_scalar(el2[:, :, :], el2[:, :, :], 1.0, None, ALU.add).then_inc(sem(rs), 1)
            dve.wait_ge(*event(rs, it, 1))
            v.reciprocal(sc2[:, :, 0:NX], el2[:, :, :]).then_inc(sem(rs), 1)
            dve.wait_ge(*event(rs, it, 2))
            carry(dve, "dve_waited")
            for t in range(T):
                v.max(m82[:, t, :], sc2[:, t, 0:NX]).then_inc(sem(rs), 1)
            dve.wait_ge(*event(rs, it, 4))
            v.memset(m82[:, :, TOP:TOP + 1], 2.0).then_inc(sem(rs), 1)
            v.memset(m82[:, :, TOP + 1:TOP + 2], 3.0).then_inc(sem(rs), 1)
            dve.wait_ge(*event(rs, it, 6))
            carry(dve, "dve_waited")
            for t in range(T):
                v.match_replace(rp2[:, t, :], m82[:, t, :], sc2[:, t, :], 0.0).then_inc(sem(rs), 1)
            dve.wait_ge(*event(rs, it, 8))
            v.tensor_tensor(cm2[:, :, :], sc2[:, :, 0:NX], rp2[:, :, 0:NX], ALU.subtract).then_inc(sem(rs), 1)
            dve.wait_ge(*event(rs, it, 9))
            v.tensor_reduce(ws2[:, :], cm2[:, :, :], AX.X, ALU.add).then_inc(sem(rs), 1)
            dve.wait_ge(*event(rs, it, 10))
            v.tensor_scalar(ws2[:, :], ws2[:, :], 1e-20, None, ALU.add).then_inc(sem(rs), 1)
            dve.wait_ge(*event(rs, it, 11))
            v.reciprocal(ws2[:, :], ws2[:, :]).then_inc(sem(rs), 1)
            dve.wait_ge(*event(rs, it, 12))
            for t in range(T):
                v.tensor_scalar(cm2[:, t, :], cm2[:, t, :], ws2[:, t:t + 1], 0.5, ALU.mult, ALU.mult).then_inc(sem(rs), 1)
            yield
            for h in range(H):
                dve.wait_ge(*full2(it, U2["q_rows"] + h))
                bk = ring2[(U2["q_rows"] + h) % 4]
                if h >= 2:
                    dve.wait_ge(*emptied2(it, U2["q_rows"] + h - 2))
                carry(dve, "dve_waited")
                v.tensor_tensor_reduce(junk2[:, h % 2, 0, 0:P], bk[:, 0:P], maskq1[:, P:S], 1.0, -3.0e38,
                                       ALU.add, ALU.max, mx2[:, h, 0:1])
                v.tensor_tensor_reduce(junk2[:, h % 2, 1, :], bk[:, S:2 * S], maskq1[:, :], 1.0, -3.0e38,
                                                ALU.add, ALU.max, mx2[:, h, 1:2]).then_inc(empties2(U2["q_rows"] + h), 1)
                yield
            dve.wait_ge(*full2(it, U2["max"]))
            bk = ring2[U2["max"] % 4]
            v.tensor_scalar(mt2[:, :], bk[0:2 * H, 0:P], -1.0, None, ALU.mult).then_inc(empties2(U2["max"]), 1)
            yield
            for h in range(HG):
                yield
            for half in range(2):
                dve.wait_ge(*event("p2_used", it, HG * (half + 1)))
                hs = slice(HG * half, HG * half + HG)
                for n, ins in normalise(dve, it, acc2, half, rc2, [on2[:, j, hs, :] for j in range(T)], "rc2_made"):
                    if n == T - 1:
                        ins.then_inc(sem("acc2_free"), 1)
                if half == 0:
                    for h in range(HG, H):
                        yield
            yield
            dve.wait_ge(*full2(it, U2["o"]))
            bk = ring2[U2["o"] % 4]
            dve.wait_ge(*event("o2h_made", it, 1))
            v.tensor_tensor(o2l, two(bk), o2h, ALU.subtract).then_inc(empties2(U2["o"]), 1)
            for n in range(UNITS + 2):
                if n >= 2:
                    m, w = unit(n - 2)
                    s = n % 2
                    dve.wait_ge(*event("h2h_made", it, n - 1))
                    dve.wait_ge(*event("down2_done", it, n - 3))
                    v.tensor_tensor(h2l[0:m, s, 0:w], th2[0:m, s, 0:w], h2h[0:m, s, 0:w], ALU.subtract).then_inc(sem("h2l_made"), 1)
                if n < UNITS:
                    m, w = unit(n)
                    s, u = n % 2, U2["unit"] + 2 * n
                    dve.wait_ge(*event("th2_made", it, n + 1))
                    dve.wait_ge(*event("gc2_made", it, n - 3 if n >= 4 else 0))
                    ins = v.scalar_tensor_tensor(gs2[0:m, s, 0:w], th2[0:m, s, 0:w], 1.0, ring2[u % 4][0:m, 0:w], ALU.add, ALU.mult)
                    ins.then_inc(empties2(u), 1)
                if 1 <= n <= UNITS:
                    m, w = unit(n - 1)
                    s, u = (n - 1) % 2, U2["unit"] + 2 * (n - 1) + 1
                    dve.wait_ge(*full2(it, u))
                    bk = ring2[u % 4]
                    if n - 1 < 2:
                        dve.wait_ge(*emptied2(it, u - 1))
                        ins = v.scalar_tensor_tensor(th2[0:m, s, 0:w], bk[0:m, 0:w], 0.5, gs2[0:m, s, 0:w], ALU.mult, ALU.mult)
                    else:
                        dve.wait_ge(*event("gc2_made", it, n - 2))
                        ins = v.tensor_tensor(th2[0:m, s, 0:w], bk[0:m, 0:w], gc2[0:m, s, 0:w], ALU.mult)
                    ins.then_inc(empties2(u), 1)
                if n < UNITS:
                    yield
            dve.wait_ge(*event("acc2_full", it, 1))
            v.tensor_tensor(xo2[:, :, :], two(acc2), xb2[:, :, :], ALU.add).then_inc(sem("acc2_free"), 1)

        @block.vector
        def _(dve):
            v = nc.vector
            dve.wait_ge(*event("gp_const", None, 12))
            for i in range(2):
                v.tensor_copy(order[i], order_i[i]).then_inc(sem("dve_const"), 1)
            dve.wait_ge(*event("dve_const", None, 2))
            for i in range(2):
                v.tensor_tensor_reduce(mask_tmp[i], order[i], ident[:, :], 1.0, 0.0, ALU.mult, ALU.add, pos[i]).then_inc(sem("dve_const"), 1)
            dve.wait_ge(*event("dve_const", None, 4))
            hi = 4.0 - 4 * L0_MASKED
            for i, op in enumerate((ALU.is_le, ALU.is_ge)):
                v.tensor_scalar(mask_tmp[2 * i], order[0], pos[0], hi, op, ALU.mult).then_inc(sem("dve_const"), 1)
                v.tensor_scalar(mask_tmp[2 * i + 1], order[1], pos[1], BIG, op, ALU.mult).then_inc(sem("dve_const"), 1)
            v.memset(maskq0[:, 0, P:S], 4 * L0_MASKED).then_inc(sem("dve_const"), 1)
            v.memset(maskq0[:, 1, 0:P], 4.0).then_inc(sem("dve_const"), 1)
            v.memset(maskq1[:, 0:P], 0.0).then_inc(sem("dve_const"), 1)
            dve.wait_ge(*event("dve_const", None, 11))
            for dst in (maskq0[:, 0, 0:P], maskq0[:, 1, P:S]):
                v.tensor_scalar(dst, mask_tmp[0], 4 * L0_MASKED, None, ALU.add).then_inc(sem("dve_const"), 1)
            v.tensor_scalar(maskq1[:, P:S], mask_tmp[1], -BIG, None, ALU.add).then_inc(sem("dve_const"), 1)
            v.tensor_scalar(maskk0[:, :], mask_tmp[2], 4 * L0_MASKED, None, ALU.add).then_inc(sem("dve_const"), 1)
            v.tensor_scalar(maskk1[:, :], mask_tmp[3], -BIG, None, ALU.add).then_inc(sem("dve_const"), 1)
            v.tensor_copy(ident16[:, :], ident[:, :]).then_inc(sem("dve_const"), 1)
            v.tensor_copy(identb[:, :], ident[:, :]).then_inc(sem("dve_const"), 1)
            v.tensor_scalar(centre[:, :], ident[0:L, 0:L], 1.0 / L, None, ALU.subtract).then_inc(sem("dve_const"), 1)
            v.tensor_scalar(head_mean[:, :], same_head[:, :, :].rearrange("p a b -> p (a b)"), 1.0 / L, None, ALU.mult).then_inc(sem("dve_const"), 1)
            v.tensor_scalar(head_mean8[:, :], same_head[:, :, 0], 1.0 / L, None, ALU.mult).then_inc(sem("dve_const"), 1)
            dve.wait_ge(*event("small_loaded", None, SMALL))
            v.tensor_scalar(sg_half[:, 0:NCH - 1], sg_half[:, 0:NCH - 1], 0.5, None, ALU.mult).then_inc(sem("dve_const"), 1)
            v.tensor_scalar(sg_half[0:CH_M[-1], NCH - 1:NCH], sg_half[0:CH_M[-1], NCH - 1:NCH], 0.5, None, ALU.mult).then_inc(sem("dve_const"), 1)
            dve.wait_ge(*event("dve_const", None, 23))
            v.tensor_tensor(su_half[:, 0:NCH - 1], su_half[:, 0:NCH - 1], sg_half[:, 0:NCH - 1], ALU.mult).then_inc(sem("dve_const"), 1)
            v.tensor_tensor(su_half[0:CH_M[-1], NCH - 1:NCH], su_half[0:CH_M[-1], NCH - 1:NCH],
                                 sg_half[0:CH_M[-1], NCH - 1:NCH], ALU.mult).then_inc(sem("dve_const"), 1)

            for i in range(NCODE):
                dve.wait_ge(*event(f"codes_loaded{i % 2}", None, 16 * (i // 2 + 1)))
                if i >= 2:
                    dve.wait_ge(*event("codes_turned", None, i - 1))
                m, n = code_size(i)
                v.tensor_scalar(code_f[i % 2][0:m, 0:n], codes[i % 2][0:m, 0:n], CODE_ZERO, None, ALU.subtract).then_inc(sem("codes_used"), 1)

            for k in range(K):
                at, fe = FD * k, "fold_dve"
                dve.wait_ge(*event("fold_pe", None, 3 * k + 1))
                v.tensor_copy(f_t[:, 0:3 * P], ring2[0][:, 0:3 * P]).then_inc(sem(fe), 1)
                dve.wait_ge(*event("fold_pe", None, 3 * k + 2))
                v.tensor_copy(f_a[0:L, 0:3 * P], ring2[1][0:L, 0:3 * P]).then_inc(sem(fe), 1)
                dve.wait_ge(*event(fe, None, at + 2))
                for w, ln in ((b_w, ln_b), (g_w, ln_g)):
                    by = ln[:, 8 * k:8 * k + 8].unsqueeze(2).to_broadcast([L, 8, HD])
                    for i in range(2):
                        v.tensor_tensor(w[:, P * i:P * i + P].rearrange("l (h d) -> l h d", h=8),
                                             f_a[0:L, P * i:P * i + P].rearrange("l (h d) -> l h d", h=8), by, ALU.mult).then_inc(sem(fe), 1)
                dve.wait_ge(*event("fold_pe", None, 3 * k + 3))
                if k:
                    dve.wait_ge(*event("fold_act", None, k))
                    dve.wait_ge(*event(fe, None, at))
                v.tensor_tensor(f_m[:, 0:3 * P].rearrange("p (a b) -> p a b", a=3),
                                     ring2[2][:, 0:3 * P].rearrange("p (a b) -> p a b", a=3),
                                     same_head[:, :, :].rearrange("p a b -> p (a b)").unsqueeze(1).to_broadcast([P, 3, P]),
                                     ALU.mult).then_inc(sem(fe), 1)
                v.tensor_copy(val_const[:, P * k:P * k + P], ring2[3][:, 0:P]).then_inc(sem(fe), 1)
                v.tensor_copy(key_const[:, k:k + 1], ring2[3][:, P:P + 1]).then_inc(sem(fe), 1)
                dve.wait_ge(*event("fold_act", None, k + 1))
                v.tensor_tensor(fold[1][:, k, :, :].rearrange("p a b -> p (a b)"), f_m[:, 0:3 * P],
                                     fold[0][:, k, :, :].rearrange("p a b -> p (a b)"), ALU.subtract).then_inc(sem(fe), 1)
            dve.wait_ge(*event("fold_act", None, K + 1))
            v.tensor_tensor(wo[1][:, :, :], two(ring2[0]), wo[0][:, :, :], ALU.subtract).then_inc(sem("fold_dve"), 1)

            for i, (src, dst, n) in enumerate(pieces):
                dve.wait_ge(*event("high_made", None, i + 1))
                v.tensor_tensor(dst[1], staged(i, n, dst[0]), dst[0], ALU.subtract).then_inc(sem("stage_free"), 1)
            run(None, dve1(dve, 0))
            with dve.Fori(1, B) as it:
                run(dve2(dve, Before(it)), dve1(dve, it))
            run(dve2(dve, B - 1), None)

        def parts3(bk, lhs, rhs, chain=None):
            n = len(lhs[0])
            terms = [(i, j, k) for i, j in ((0, 0), (0, 1), (1, 0)) for k in range(n)]
            for x, (i, j, k) in enumerate(terms):
                first, last = x == 0, x == len(terms) - 1
                if chain:
                    ins = nc.tensor.matmul(bk, lhs[i][k], rhs[j][k], start=first and chain[0], stop=last and chain[1],
                                           skip_group_check=True)
                else:
                    ins = nc.tensor.matmul(bk, lhs[i][k], rhs[j][k], start=first, stop=last)
            return ins

        def turn(pe, bk, x, chunk):
            for k in range(K):
                for t in range(T):
                    ins = nc.tensor.transpose(two(bk)[:, k, P * t:P * t + P], chunk(x, t, k), ident[:, :])
            return ins

        def tok(x, t):
            return [w[:, k, P * t:P * t + P] for w in x for k in range(K)]

        def pe1(pe, it):
            mm = nc.tensor.matmul
            xh, xl = x1h, x1l
            xp = [[x[:, k, :] for k in range(K)] for x in (x1h, x1l)]
            xt = [[[x[:, k, P * t:P * t + P] for k in range(K)] for x in (x1h, x1l)] for t in range(T)]
            pe.wait_ge(*event("ln1", it, 8))
            pe.wait_ge(*free1(it, U1["x"]))
            bk = ring1[U1["x"] % 2]
            turn(pe, bk, xn1, lambda x, t, k: x[:, t, P * k:P * k + P]).then_inc(fills1(U1["x"]), 1)
            pe.wait_ge(*emptied1(it, U1["x"]))
            yield
            for i, u in enumerate(("q", "k")):
                pe.wait_ge(*free1(it, U1[u]))
                bk = ring1[U1[u] % 2]
                for m in range(K):
                    col = E * i + P * m
                    ins = parts3(two(bk)[:, m, :], [[w[:, k, col:col + P] for k in range(K)] for w in wqkv], xp)
                ins.then_inc(fills1(U1[u]), 1)
            yield
            pe.wait_ge(*free1(it, U1["v"]))
            bk = ring1[U1["v"] % 2]
            for t in range(T):
                ins = parts3(two(bk)[:, t, :], xt[t], [[w[:, k, 2 * E:3 * E] for k in range(K)] for w in wqkv])
            ins.then_inc(fills1(U1["v"]), 1)

            def ffn(c):
                m = CH_M[c]
                for i, w in enumerate((wgate, wup)):
                    pe.wait_ge(*free1(it, ffn_use(c) + i))
                    bk = ring1[(ffn_use(c) + i) % 2]
                    for x in range(2):
                        for k in range(K):
                            ins = mm(bk[0:m, 0:S], w[:, k, P * c:P * c + m], xp[x][k], start=(x + k == 0), stop=(x + k == K))
                    ins.then_inc(fills1(ffn_use(c) + i), 1)

            def down(c):
                m = CH_M[c]
                pe.wait_ge(*event("h1l_made", it, c + 1))
                if c == 0:
                    pe.wait_ge(*event("acc1_free", it, 0))
                for t in range(T):
                    for i, hp in enumerate((h1h, h1l)):
                        ins = mm(two(acc1)[:, t, :], hp[0:m, c % 2, P * t:P * t + P], wdown[0:m, c, :],
                                 start=(c + t + i == 0), stop=(c == NCH - 1 and i == 1), skip_group_check=True)
                ins.then_inc(sem("down1_done"), 1)

            for c in range(3):
                ffn(c)
                if c:
                    down(c - 1)
                yield
            down(2)
            pe.wait_ge(*event("stack1_made", it, 2))
            for h in range(H):
                pe.wait_ge(*free1(it, U1["q_rows"] + h))
                bk = ring1[(U1["q_rows"] + h) % 2]
                for j in range(T):
                    ins = mm(two(bk)[:, j, :], qst1[0:3 * HD, h, P * j:P * j + P], kst1[0:3 * HD, h, :], start=True, stop=True)
                ins.then_inc(fills1(U1["q_rows"] + h), 1)
                yield
            pe.wait_ge(*emptied1(it, U1["q_rows"] + H - 1))
            pe.wait_ge(*free1(it, U1["max"]))
            bk = ring1[U1["max"] % 2]
            nc.tensor.transpose(bk[0:2 * H, 0:P], mx1[:, :, :].rearrange("p h j -> p (h j)"), ident[:, :]).then_inc(fills1(U1["max"]), 1)
            for c in range(3, NCH):
                ffn(c)
                if c > 3:
                    down(c - 1)
                yield
            down(NCH - 1)
            pe.wait_ge(*event("max1_placed", it, 16))
            pe.wait_ge(*event("va1_loaded", it, 16 * C * T))
            for h in range(H + 1):
                if h < H:
                    pe.wait_ge(*free1(it, U1["k_rows"] + h))
                    bk = ring1[(U1["k_rows"] + h) % 2]
                    for j in range(T):
                        mm(two(bk)[:, j, :], kst1[0:QK0, h, P * j:P * j + P], qst1[0:QK0, h, :], start=True, stop=False)
                        ins = mm(two(bk)[:, j, P * j:P * j + P], ident16[:, :], maskk0[:, :], start=False, stop=True)
                    ins.then_inc(fills1(U1["k_rows"] + h), 1)
                if h >= 1:
                    g = h - 1
                    if g % HG == 0:
                        pe.wait_ge(*event("acc1_free", it, 1 + g // HG))
                    pe.wait_ge(*emptied1(it, U1["k_rows"] + g))
                    for j in range(T):
                        at = (g % HG) * 2 * (HD + 1) + j * (HD + 1)
                        for kc in range(2):
                            ins = mm(acc1[:, at:at + HD + 1], p1[:, g % 2, kc, P * j:P * j + P], va1[:, kc, g, :],
                                     start=(kc == 0), stop=(kc == 1))
                    ins.then_inc(sem("p1_used"), 1)
                yield
            pe.wait_ge(*event("ot1_loaded", it, 16))
            pe.wait_ge(*free1(it, U1["o"]))
            bk = ring1[U1["o"] % 2]
            turn(pe, bk, ot1, lambda x, t, k: x[:, t, P * k:P * k + P]).then_inc(fills1(U1["o"]), 1)
            pe.wait_ge(*emptied1(it, U1["o"]))
            pe.wait_ge(*event("acc1_free", it, 3))
            for t in range(T):
                ins = parts3(two(acc1)[:, t, :], [[x[:, k, P * t:P * t + P] for k in range(K)] for x in (o1h, o1l)],
                             [[w[:, k, :] for k in range(K)] for w in wout])
            ins.then_inc(sem("acc1_full"), 1)

        def pe2(pe, it):
            mm = nc.tensor.matmul
            x2p = (x2h, x2l)
            xp = [[x[:, k, :] for k in range(K)] for x in x2p]
            xt = [[[x[:, k, P * t:P * t + P] for k in range(K)] for x in x2p] for t in range(T)]
            pe.wait_ge(*event("ln2", it, 8))
            pe.wait_ge(*free2(it, U2["x"]))
            bk = ring2[U2["x"] % 4]
            turn(pe, bk, xn2, lambda x, t, k: x[:, t, P * k:P * k + P]).then_inc(fills2(U2["x"]), 1)
            pe.wait_ge(*emptied2(it, U2["x"]))
            yield
            pe.wait_ge(*free2(it, U2["gram"]))
            bk = ring2[U2["gram"] % 4]
            for k in range(K):
                ins = parts3(two(bk)[:, k, :], [[f[:, k, 2, :]] for f in fold], [[x[:, k, :]] for x in x2p])
            ins.then_inc(fills2(U2["gram"]), 1)
            pe.wait_ge(*emptied2(it, U2["gram"]))
            pe.wait_ge(*free2(it, U2["var"]))
            bk = ring2[U2["var"] % 4]
            for k in range(K):
                ins = mm(two(bk)[:, k, :], head_mean[:, :], pr2[:, k, :], start=True, stop=True)
            ins.then_inc(fills2(U2["var"]), 1)
            pe.wait_ge(*free2(it, U2["var_t"]))
            bk = ring2[U2["var_t"] % 4]
            for t in range(T):
                for k in range(K):
                    at = H * t + 8 * k
                    ins = mm(bk[:, at:at + 8], pr2[:, k, P * t:P * t + P], head_mean8[:, :], start=True, stop=True)
            ins.then_inc(fills2(U2["var_t"]), 1)
            yield
            pe.wait_ge(*free2(it, U2["k"]))
            bk = ring2[U2["k"] % 4]
            for k in range(K):
                ins = parts3(two(bk)[:, k, :], [[f[:, k, 0, :]] for f in fold], [[x[:, k, :]] for x in x2p])
            ins.then_inc(fills2(U2["k"]), 1)
            pe.wait_ge(*free2(it, U2["v"]))
            bk = ring2[U2["v"] % 4]
            for t in range(T):
                for k in range(K):
                    ins = parts3(two(bk)[:, t, P * k:P * k + P], [[x[k]] for x in xt[t]], [[f[:, k, 1, :]] for f in fold])
            ins.then_inc(fills2(U2["v"]), 1)
            pe.wait_ge(*free2(it, U2["logit"]))
            bk = ring2[U2["logit"] % 4]
            for t in range(T):
                ins = parts3(bk[:, NX * t:NX * t + NX], xt[t], [[w[:, k, :] for k in range(K)] for w in rout])
            ins.then_inc(fills2(U2["logit"]), 1)
            yield
            pe.wait_ge(*event("router", it, 14))
            pe.wait_ge(*free2(it, U2["comb"]))
            bk = ring2[U2["comb"] % 4]
            for t in range(T):
                ins = nc.tensor.transpose(bk[0:NX, P * t:P * t + P], cm2[:, t, :], ident[:, :])
            ins.then_inc(fills2(U2["comb"]), 1)
            yield
            pe.wait_ge(*event("stack2_loaded", it, 96))
            for h in range(H):
                pe.wait_ge(*free2(it, U2["q_rows"] + h))
                bk = ring2[(U2["q_rows"] + h) % 4]
                for j in range(T):
                    ins = mm(bk[:, S * j:S * j + P * (j + 1)], qst2[0:3 * HD, h, P * j:P * j + P],
                             kst2[0:3 * HD, h, 0:P * (j + 1)], start=True, stop=True)
                ins.then_inc(fills2(U2["q_rows"] + h), 1)
                yield
            pe.wait_ge(*emptied2(it, U2["q_rows"] + H - 1))
            pe.wait_ge(*free2(it, U2["max"]))
            bk = ring2[U2["max"] % 4]
            nc.tensor.transpose(bk[0:2 * H, 0:P], mx2[:, :, :].rearrange("p h j -> p (h j)"), ident[:, :]).then_inc(fills2(U2["max"]), 1)
            yield
            pe.wait_ge(*event("max2_placed", it, 16))
            pe.wait_ge(*event("va2_made", it, 2))
            for h in range(H + 1):
                if h < H:
                    pe.wait_ge(*free2(it, U2["k_rows"] + h))
                    bk = ring2[(U2["k_rows"] + h) % 4]
                    for j in range(T):
                        at = S * j
                        mm(bk[:, at:at + S - P * j], kst2[0:QK1, h, P * j:P * j + P], qst2[0:QK1, h, P * j:S],
                           start=True, stop=False)
                        ins = mm(bk[:, at:at + P], identb[:, :], maskk1[:, :], start=False, stop=True)
                    ins.then_inc(fills2(U2["k_rows"] + h), 1)
                if h >= 1:
                    g = h - 1
                    if g % HG == 0:
                        pe.wait_ge(*event("acc2_free", it, g // HG))
                    pe.wait_ge(*emptied2(it, U2["k_rows"] + g))
                    at = (g % HG) * 2 * (HD + 1)
                    mm(acc2[:, at:at + HD + 1], p2[:, g % 2, 0:P], va2[:, 0, g, :], start=True, stop=True)
                    at += HD + 1
                    mm(acc2[:, at:at + HD + 1], p2[:, g % 2, P:2 * P], va2[:, 0, g, :], start=True, stop=False)
                    mm(acc2[:, at:at + HD + 1], p2[:, g % 2, 2 * P:3 * P], va2[:, 1, g, :], start=False, stop=True).then_inc(sem("p2_used"), 1)
                yield
            pe.wait_ge(*event("acc2_free", it, 2))
            pe.wait_ge(*free2(it, U2["o"]))
            bk = ring2[U2["o"] % 4]
            turn(pe, bk, on2, lambda x, t, k: x[:, t, 8 * k:8 * k + 8, :].rearrange("p h d -> p (h d)")).then_inc(fills2(U2["o"]), 1)

            def gate_up(n):
                m, w = unit(n)
                for i in range(2):
                    u = U2["unit"] + 2 * n + i
                    pe.wait_ge(*free2(it, u))
                    bk = ring2[u % 4]
                    ws, c = ((shg, shu)[i], n) if n < 2 else ((xg, xu)[i], 2 * (n - 2))
                    for q in range(w // S):
                        ins = parts3(bk[0:m, S * q:S * q + S], [[x[:, k, P * (c + q):P * (c + q) + m] for k in range(K)] for x in ws], xp)
                    ins.then_inc(fills2(u), 1)

            def down(n):
                m, w = unit(n)
                pe.wait_ge(*event("h2l_made", it, n + 1))
                for q in range(w // S):
                    ws, c = (shd, n) if n < 2 else (xd, 2 * (n - 2) + q)
                    for t in range(T):
                        hs = [[x[0:m, n % 2, S * q + P * t:S * q + P * t + P]] for x in (h2h, h2l)]
                        ins = parts3(two(acc2)[:, t, :], hs, [[x[0:m, c, :]] for x in ws], chain=(n + t == 0, False))
                ins.then_inc(sem("down2_done"), 1)

            for n in range(UNITS + 2):
                if n < UNITS:
                    gate_up(n)
                if n >= 2:
                    down(n - 2)
                if n < UNITS:
                    yield
            pe.wait_ge(*emptied2(it, U2["o"]))
            for t in range(T):
                ins = parts3(two(acc2)[:, t, :], [[x[:, k, P * t:P * t + P] for k in range(K)] for x in (o2h, o2l)],
                             [[w[:, k, :] for k in range(K)] for w in wo], chain=(False, True))
            ins.then_inc(sem("acc2_full"), 1)

        @block.tensor
        def _(pe):
            mm, tr = nc.tensor.matmul, nc.tensor.transpose
            pe.wait_ge(*event("dve_const", None, 21))
            for i in range(NCODE):
                pe.wait_ge(*event("codes_used", None, i + 1))
                if i >= 2:
                    pe.wait_ge(*event("codes_kept", None, i - 1))
                bk, f = ring1[i % 2], code_f[i % 2]
                m, n = code_size(i)
                if i < 2 * NCH:
                    for k in range(K):
                        ins = tr(bk[:, 256 * k:256 * k + m], f[0:m, P * k:P * k + P], ident[0:m, 0:m])
                else:
                    for b in range(2):
                        w = min(P, n - P * b)
                        ins = tr(bk[0:w, 256 * b:256 * b + P], f[:, P * b:P * b + w], ident[:, :])
                ins.then_inc(sem("codes_turned"), 1)
            pe.wait_ge(*event("small_loaded", None, SMALL))
            for k in range(K):
                if k:
                    pe.wait_ge(*event("fold_dve", None, FD * k))
                bk, cs = ring2[0], slice(P * k, P * k + P)
                tr(bk[:, 0:P], wq_bd[:, k, 0:P], ident[:, :])
                tr(bk[:, P:2 * P], wo_bd[:, k, 0:P], ident[:, :])
                tr(bk[:, 2 * P:2 * P + L], wuk[:, cs], ident[0:L, 0:L])
                tr(bk[:, 2 * P + L:3 * P], wuv[:, cs], ident[0:L, 0:L]).then_inc(sem("fold_pe"), 1)
                pe.wait_ge(*event("fold_dve", None, FD * k + 1))
                bk = ring2[1][0:L]
                mm(bk[:, 0:P], f_t[:, 2 * P:2 * P + L], f_t[:, 0:P], start=True, stop=True)
                mm(bk[:, P:2 * P], f_t[:, 2 * P + L:3 * P], f_t[:, P:2 * P], start=True, stop=True)
                mm(bk[:, 2 * P:3 * P], centre[:, :], wdkv[:, cs], start=True, stop=True).then_inc(sem("fold_pe"), 1)
                pe.wait_ge(*event("fold_dve", None, FD * k + 6))
                wc = f_a[0:L, 2 * P:3 * P]
                for i, r in enumerate((g_w[:, 0:P], g_w[:, P:2 * P], wc)):
                    mm(ring2[2][:, P * i:P * i + P], wc, r, start=True, stop=True)
                mm(ring2[3][:, 0:P], one64[:, :], b_w[:, P:2 * P], start=True, stop=True)
                mm(ring2[3][:, P:P + 1], b_w[:, 0:P], one64[:, 0:1], start=True, stop=True).then_inc(sem("fold_pe"), 1)
            pe.wait_ge(*event("fold_dve", None, FD * K))
            for k in range(K):
                for m in range(K):
                    ins = tr(two(ring2[0])[:, k, P * m:P * m + P], wo_nat[:, m, P * k:P * k + P], ident[:, :])
            ins.then_inc(sem("fold_pe"), 1)
            pe.wait_ge(*event("fold_dve", None, FD * K + 1))
            pe.wait_ge(*event("codes_kept", None, NCODE))
            pe.wait_ge(*event("stage_free", None, len(pieces)))
            run(None, pe1(pe, 0))
            with pe.Fori(1, B) as it:
                run(pe2(pe, Before(it)), pe1(pe, it))
            run(pe2(pe, B - 1), None)


INS = ["L0_attn_x", "L0_attn_w_qkv", "L0_attn_w_out", "L0_ffn_wq_gate", "L0_ffn_s_gate", "L0_ffn_wq_up", "L0_ffn_s_up",
       "L0_ffn_wq_down", "L0_ffn_s_down", "L1_attn_Wq", "L1_attn_Wdkv", "L1_attn_Wuk", "L1_attn_Wuv", "L1_attn_ln_g",
       "L1_attn_ln_b", "L1_attn_Wo_h", "L1_attn_Wo", "L1_attn_bo", "L1_ffn_gate_w", "L1_ffn_wg", "L1_ffn_wu", "L1_ffn_wd",
       "L1_ffn_sg", "L1_ffn_su", "L1_ffn_sd"]


def kernel(**inputs):
    import concourse.bacc as _bacc
    from concourse.bass_utils import run_bass_kernel_spmd as _run

    nc = _bacc.Bacc("TRN2", target_bir_lowering=False, num_devices=1)
    arrays, aps = {}, {}
    for name in INS:
        x = np.ascontiguousarray(inputs[name])
        arrays[f"in_{name}"] = x
        aps[name] = nc.dram_tensor(f"in_{name}", x.shape, mybir.dt.from_np(x.dtype), kind="ExternalInput").ap()
    shape = inputs["L0_attn_x"].shape
    out = nc.dram_tensor("out", shape, F32, kind="ExternalOutput").ap()
    program(nc, aps, out)
    return _run(nc, [arrays], core_ids=[0]).results[0]["out"]
```
